# Optimizing a Trainium2 kernel written in Bass

```python
import numpy as np
import jax
import jax.numpy as jnp

def _softmax(x, axis=-1):
    return jax.nn.softmax(x, axis=axis)

def _gelu(x):
    return jax.nn.gelu(x, approximate=True)

def _silu(x):
    return jax.nn.silu(x)

def _sigmoid(x):
    return jax.nn.sigmoid(x)

def _layernorm(x, axis=-1, eps=1e-05):
    m = jnp.mean(x, axis=axis, keepdims=True)
    v = jnp.var(x, axis=axis, keepdims=True)
    return (x - m) / jnp.sqrt(v + eps)

def _scatter_add(tgt, idx, src, axis=0):
    return tgt.at[idx].add(src)

def _segment_sum(src, seg, n):
    return jax.ops.segment_sum(src, seg, n)
kernel_name = 'mk_rec_standalone_d1_rec_r8_170cd6'

def setup_inputs(seed: int=0):
    np.random.seed(seed)
    _w = jnp.asarray

    def _rec_inputs():
        import jax
        import jax.numpy as jnp
        _rk = jax.random.key(seed)
        r_numerical = 8.7408e-05 + 1.0001 * jax.random.normal(jax.random.fold_in(_rk, 1), (512, 13), jnp.float32)
        r_cat_features = jnp.stack([jax.random.randint(jax.random.fold_in(jax.random.fold_in(_rk, 2), 0), (512,), 2, 12500, jnp.int32), jax.random.randint(jax.random.fold_in(jax.random.fold_in(_rk, 2), 1), (512,), 1, 99999, jnp.int32), jax.random.randint(jax.random.fold_in(jax.random.fold_in(_rk, 2), 2), (512,), 0, 12500, jnp.int32), jax.random.randint(jax.random.fold_in(jax.random.fold_in(_rk, 2), 3), (512,), 0, 12500, jnp.int32), jax.random.randint(jax.random.fold_in(jax.random.fold_in(_rk, 2), 4), (512,), 10, 99997, jnp.int32), jax.random.randint(jax.random.fold_in(jax.random.fold_in(_rk, 2), 5), (512,), 0, 99993, jnp.int32), jax.random.randint(jax.random.fold_in(jax.random.fold_in(_rk, 2), 6), (512,), 2, 99999, jnp.int32), jax.random.randint(jax.random.fold_in(jax.random.fold_in(_rk, 2), 7), (512,), 1, 99995, jnp.int32), jax.random.randint(jax.random.fold_in(jax.random.fold_in(_rk, 2), 8), (512,), 0, 12500, jnp.int32), jax.random.randint(jax.random.fold_in(jax.random.fold_in(_rk, 2), 9), (512,), 2, 99999, jnp.int32), jax.random.randint(jax.random.fold_in(jax.random.fold_in(_rk, 2), 10), (512,), 0, 99999, jnp.int32), jax.random.randint(jax.random.fold_in(jax.random.fold_in(_rk, 2), 11), (512,), 6, 99999, jnp.int32), jax.random.randint(jax.random.fold_in(jax.random.fold_in(_rk, 2), 12), (512,), 0, 99999, jnp.int32), jax.random.randint(jax.random.fold_in(jax.random.fold_in(_rk, 2), 13), (512,), 3, 99996, jnp.int32), jax.random.randint(jax.random.fold_in(jax.random.fold_in(_rk, 2), 14), (512,), 0, 99999, jnp.int32), jax.random.randint(jax.random.fold_in(jax.random.fold_in(_rk, 2), 15), (512,), 3, 99997, jnp.int32), jax.random.randint(jax.random.fold_in(jax.random.fold_in(_rk, 2), 16), (512,), 0, 99999, jnp.int32), jax.random.randint(jax.random.fold_in(jax.random.fold_in(_rk, 2), 17), (512,), 0, 99998, jnp.int32), jax.random.randint(jax.random.fold_in(jax.random.fold_in(_rk, 2), 18), (512,), 10, 99997, jnp.int32), jax.random.randint(jax.random.fold_in(jax.random.fold_in(_rk, 2), 19), (512,), 0, 99999, jnp.int32), jax.random.randint(jax.random.fold_in(jax.random.fold_in(_rk, 2), 20), (512,), 0, 12500, jnp.int32), jax.random.randint(jax.random.fold_in(jax.random.fold_in(_rk, 2), 21), (512,), 1, 12500, jnp.int32), jax.random.randint(jax.random.fold_in(jax.random.fold_in(_rk, 2), 22), (512,), 1, 99997, jnp.int32), jax.random.randint(jax.random.fold_in(jax.random.fold_in(_rk, 2), 23), (512,), 2, 12500, jnp.int32), jax.random.randint(jax.random.fold_in(jax.random.fold_in(_rk, 2), 24), (512,), 1, 12500, jnp.int32), jax.random.randint(jax.random.fold_in(jax.random.fold_in(_rk, 2), 25), (512,), 2, 99995, jnp.int32)], axis=1)
        return (r_numerical, r_cat_features)
    r_numerical, r_cat_features = _rec_inputs()

    def _L0_rec_setup():
        import jax, jax.numpy as jnp
        import numpy as np
        B = 4096
        NUM_DENSE = 13
        PAD_DENSE = 16
        T = 26
        V = 12500
        E = 128
        BOTTOM_DIMS = [512, 256, 128]
        TOP_DIMS = [1024, 1024, 512, 256, 1]
        N_FEAT = T + 1
        PAIR = N_FEAT * (N_FEAT - 1) // 2
        TOP_IN = PAIR + E
        TOP_PAD = 480

        def _glorot(key, fan_in, fan_out):
            s = np.sqrt(2.0 / (fan_in + fan_out))
            return jax.random.normal(key, (fan_in, fan_out), jnp.float32) * s
        key = jax.random.key(seed)
        ks = jax.random.split(key, 32)
        inp = {'numerical': jax.random.normal(ks[0], (B, NUM_DENSE), jnp.float32), 'cat_features': jax.random.randint(ks[1], (B, T), 0, V, jnp.int32), 'emb_tables': jax.random.normal(ks[2], (T, V, E), jnp.float32) * 0.01}
        d_in = PAD_DENSE
        for i, d in enumerate(BOTTOM_DIMS):
            inp[f'bw{i}'] = _glorot(ks[3 + 2 * i], d_in, d)
            inp[f'bb{i}'] = jax.random.normal(ks[4 + 2 * i], (d,), jnp.float32) * np.sqrt(1.0 / d)
            d_in = d
        d_in = TOP_PAD
        for i, d in enumerate(TOP_DIMS):
            inp[f'tw{i}'] = _glorot(ks[12 + 2 * i], d_in, d)
            inp[f'tb{i}'] = jax.random.normal(ks[13 + 2 * i], (d,), jnp.float32) * np.sqrt(1.0 / d)
            d_in = d
        return inp
    _L0_rec_all = _L0_rec_setup()
    _L0_rec_in = {k: v for k, v in _L0_rec_all.items() if k in ('emb_tables', 'bw0', 'bb0', 'bw1', 'bb1', 'bw2', 'bb2', 'tw0', 'tb0', 'tw1', 'tb1', 'tw2', 'tb2', 'tw3', 'tb3', 'tw4', 'tb4')}
    del _L0_rec_all
    return {'r_numerical': r_numerical, 'r_cat_features': r_cat_features, 'L0_rec_emb_tables': _L0_rec_in['emb_tables'], 'L0_rec_bw0': _L0_rec_in['bw0'], 'L0_rec_bb0': _L0_rec_in['bb0'], 'L0_rec_bw1': _L0_rec_in['bw1'], 'L0_rec_bb1': _L0_rec_in['bb1'], 'L0_rec_bw2': _L0_rec_in['bw2'], 'L0_rec_bb2': _L0_rec_in['bb2'], 'L0_rec_tw0': _L0_rec_in['tw0'], 'L0_rec_tb0': _L0_rec_in['tb0'], 'L0_rec_tw1': _L0_rec_in['tw1'], 'L0_rec_tb1': _L0_rec_in['tb1'], 'L0_rec_tw2': _L0_rec_in['tw2'], 'L0_rec_tb2': _L0_rec_in['tb2'], 'L0_rec_tw3': _L0_rec_in['tw3'], 'L0_rec_tb3': _L0_rec_in['tb3'], 'L0_rec_tw4': _L0_rec_in['tw4'], 'L0_rec_tb4': _L0_rec_in['tb4']}

def reference(r_numerical, r_cat_features, L0_rec_emb_tables, L0_rec_bw0, L0_rec_bb0, L0_rec_bw1, L0_rec_bb1, L0_rec_bw2, L0_rec_bb2, L0_rec_tw0, L0_rec_tb0, L0_rec_tw1, L0_rec_tb1, L0_rec_tw2, L0_rec_tb2, L0_rec_tw3, L0_rec_tb3, L0_rec_tw4, L0_rec_tb4):
    import jax
    import jax.numpy as jnp

    def _L0_rec_ref(numerical, cat_features, emb_tables, bw0, bb0, bw1, bb1, bw2, bb2, tw0, tb0, tw1, tb1, tw2, tb2, tw3, tb3, tw4, tb4):
        import jax, jax.numpy as jnp
        import numpy as np
        B = 4096
        NUM_DENSE = 13
        PAD_DENSE = 16
        T = 26
        V = 12500
        E = 128
        BOTTOM_DIMS = [512, 256, 128]
        TOP_DIMS = [1024, 1024, 512, 256, 1]
        N_FEAT = T + 1
        PAIR = N_FEAT * (N_FEAT - 1) // 2
        TOP_IN = PAIR + E
        TOP_PAD = 480

        def _glorot(key, fan_in, fan_out):
            s = np.sqrt(2.0 / (fan_in + fan_out))
            return jax.random.normal(key, (fan_in, fan_out), jnp.float32) * s
        b = numerical.shape[0]
        x = jnp.pad(numerical, ((0, 0), (0, PAD_DENSE - NUM_DENSE)))
        for w, bias in ((bw0, bb0), (bw1, bb1), (bw2, bb2)):
            x = jax.nn.relu(x @ w + bias)
        bottom_out = x
        emb_out = jax.vmap(lambda tab, idx: tab[idx], in_axes=(0, 1), out_axes=1)(emb_tables, cat_features)
        feats = jnp.concatenate([bottom_out[:, None, :], emb_out], axis=1)
        Z = jnp.einsum('bnd,bmd->bnm', feats, feats)
        iu, ju = jnp.triu_indices(N_FEAT, k=1)
        pair = Z[:, iu, ju]
        x = jnp.concatenate([bottom_out, pair, jnp.zeros((b, TOP_PAD - TOP_IN), feats.dtype)], axis=1)
        tops = ((tw0, tb0), (tw1, tb1), (tw2, tb2), (tw3, tb3), (tw4, tb4))
        for i, (w, bias) in enumerate(tops):
            x = x @ w + bias
            if i < len(tops) - 1:
                x = jax.nn.relu(x)
        return x
    y = _L0_rec_ref(r_numerical, r_cat_features, L0_rec_emb_tables, L0_rec_bw0, L0_rec_bb0, L0_rec_bw1, L0_rec_bb1, L0_rec_bw2, L0_rec_bb2, L0_rec_tw0, L0_rec_tb0, L0_rec_tw1, L0_rec_tb1, L0_rec_tw2, L0_rec_tb2, L0_rec_tw3, L0_rec_tb3, L0_rec_tw4, L0_rec_tb4)
    return y

_drawn_inputs = setup_inputs


def setup_inputs(seed=0):
    import zlib

    import numpy as np

    out = dict(_drawn_inputs(seed))
    spreads = {}
    factors = {}
    for name, (base, spread) in spreads.items():
        noise = np.random.default_rng([zlib.crc32(name.encode()), seed]).standard_normal(out[name].shape)
        drawn = base * np.exp(spread * noise) if base else spread * noise
        out[name] = jnp.asarray(drawn.astype(out[name].dtype))
    for name, factor in factors.items():
        out[name] = (out[name] * factor).astype(out[name].dtype)
    return out
```

```python
from contextlib import ExitStack

import concourse.bass as bass
import numpy as np
from concourse import mybir

F32 = mybir.dt.float32
F32R = mybir.dt.float32r
I32 = mybir.dt.int32
U32 = mybir.dt.uint32
ALU = mybir.AluOpType
ACT = mybir.ActivationFunctionType

P = 128
B = 512
E = 128
T = 26
V = 12500
NF = T + 1
NUM_DENSE, PAD_DENSE = 13, 16
TILE = 128
TILES = B // TILE
HALF = 256
HALVES = B // HALF
TOP_PAD = 480

QUAD = 32
WIN = NF // 2
SLOTS = WIN + 1
KT = 4

BOTTOM = [(1, 4), (4, 2), (2, 1)]
TOP = [(1 + KT, 8), (8, 8), (8, 4), (4, 2)]
BIAS_COLS = [0, 4, 6, 7, 15, 23, 27, 29]

BANK_TABLES = 4
BANKS = -(-T // BANK_TABLES)
GROUP = P // QUAD
CHUNK = 8
CHUNKS = TILE // (GROUP * CHUNK)

W_RING = 4
W_AHEAD = W_RING - 1
PIECE = 1024


def bank_tables(bank):
    return range(bank * BANK_TABLES, min(T, (bank + 1) * BANK_TABLES))


def plan():
    groups, pieces = [], []
    offset = 0
    raw_at = {}
    for layer, (kt, mt) in enumerate(BOTTOM):
        pieces.append(dict(kind="bottom", layer=layer, size=kt * mt * P, at=offset, parts=PAD_DENSE if layer == 0 else P))
        offset += kt * mt * P
        for m in range(mt):
            groups.append(dict(layer=layer, m=m, half=None, piece=layer, split=True))
    for half in range(HALVES):
        for n, (kt, mt) in enumerate(TOP):
            for m in range(mt):
                groups.append(dict(layer=3 + n, m=m, half=half, piece=len(pieces), split=n < 3))
                pieces.append(dict(kind="top", layer=3 + n, size=kt * P, at=m * kt * P, parts=P))
        groups.append(dict(layer=7, m=0, half=half, piece=None, split=False))
    return groups, pieces


def dlrm(nc, cat, dense, emb, bottom_w, top_w, last_w, biases, last_bias, identity, b_mask, out):
    groups, pieces = plan()
    last_group_of_piece = {g["piece"]: i for i, g in enumerate(groups) if g["piece"] is not None}
    n_bottom = sum(mt for _, mt in BOTTOM)
    per_half = (len(groups) - n_bottom) // HALVES

    def split_groups(i):
        return sum(g["split"] for g in groups[:i])

    def group_range(half, layer):
        return [i for i, g in enumerate(groups) if g["half"] == half and g["layer"] == layer]

    ctx = ExitStack()
    with ctx:
        def sb(name, shape, dt=F32):
            return ctx.enter_context(nc.sbuf_tensor(name, shape, dt))

        def sem(name):
            return ctx.enter_context(nc.semaphore(name))

        cat_i = sb("cat_i", [P, TILES * T], I32)
        cat_f = sb("cat_f", [P, TILES * T])
        wrap = sb("wrap", [P, TILES * T])
        row_f = sb("row_f", [P, TILES * T])
        table_base = sb("table_base", [P, TILES * T], I32)
        row_index = sb("row_index", [P, TILES * T], U32)
        rows = sb("rows", [P, 2 * T, E])
        ident = sb("ident", [P, P])
        mask = sb("mask", [P, WIN, CHUNK], U32)
        bias = sb("bias", [P, BIAS_COLS[-1]])
        bias_last = sb("bias_last", [1, 1])
        feats = sb("feats", [P, QUAD, GROUP, QUAD])
        pairs = sb("pairs", [P, 2, KT, TILE])
        pairs_hi = sb("pairs_hi", [P, KT, HALF], F32R)
        pairs_lo = sb("pairs_lo", [P, KT, HALF], F32R)
        bottom_full = sb("bottom_full", [P, B])
        bottom_hi = sb("bottom_hi", [P, B], F32R)
        bottom_lo = sb("bottom_lo", [P, B], F32R)
        x_dense, x_hi, x_lo = (t[0:PAD_DENSE, :] for t in (bottom_full, bottom_hi, bottom_lo))
        even_hi = sb("even_hi", [P, 8 * HALF], F32R)
        even_lo = sb("even_lo", [P, 8 * HALF], F32R)
        odd_hi = sb("odd_hi", [P, 8 * HALF], F32R)
        odd_lo = sb("odd_lo", [P, 8 * HALF], F32R)
        full = sb("full", [P, 2, B])
        last_x = sb("last_x", [P, 2, HALF])
        logits = sb("logits", [1, B])
        raw = [sb(f"raw{n}", [P, mt * kt * P]) for n, (kt, mt) in enumerate(TOP)]
        raw_last = sb("raw_last", [P, 2])
        w_hi = sb("w_hi", [P, W_RING, PIECE], F32R)
        w_lo = sb("w_lo", [P, W_RING, PIECE], F32R)

        n_bottom_w = sum(p["size"] for p in pieces if p["kind"] == "bottom")
        bottom_slots = n_bottom_w // E
        raw_bottom = rows[:, 2 * T - bottom_slots:2 * T, :].rearrange("p t e -> p (t e)")

        turned = ctx.enter_context(nc.psum_tensor("turned", [P, 2, BANK_TABLES, TILE], F32))
        dots = ctx.enter_context(nc.psum_tensor("dots", [P, 2, CHUNK, P], F32))
        acc = ctx.enter_context(nc.psum_tensor("acc", [P, 2, B], F32))

        cat_loaded, dense_loaded, bias_loaded = sem("cat_loaded"), sem("dense_loaded"), sem("bias_loaded")
        ident_loaded, mask_loaded = sem("ident_loaded"), sem("mask_loaded")
        bottom_loaded = [sem(f"bottom{n}_loaded") for n in range(len(BOTTOM))]
        top_loaded = [sem(f"top{n}_loaded") for n in range(len(TOP))]
        last_loaded, bias_last_loaded = sem("last_loaded"), sem("bias_last_loaded")
        gathered = [sem(f"gathered{j}") for j in range(TILES * BANKS)]
        stored = sem("stored")
        base_ready = sem("base_ready")
        index_step = sem("index_step")
        zeroed = sem("zeroed")
        x_hi_ready, x_lo_ready = sem("x_hi_ready"), sem("x_lo_ready")
        w_hi_ready, w_lo_ready = sem("w_hi_ready"), sem("w_lo_ready")
        group_done = sem("group_done")
        taken = sem("taken")
        lo_ready = sem("lo_ready")
        bank_turned = sem("bank_turned")
        even_moved, odd_moved = sem("even_moved"), sem("odd_moved")
        first_moved = sem("first_moved")
        chunk_done = sem("chunk_done")
        a_moved = sem("a_moved")
        b_moved = sem("b_moved")
        pairs_hi_ready, pairs_lo_ready = sem("pairs_hi_ready"), sem("pairs_lo_ready")

        def result_hi_lo(g):
            layer, m, half = g["layer"], g["m"], g["half"]
            n = B if half is None else HALF
            if layer == 2:
                return bottom_hi[:, :], bottom_lo[:, :]
            hi, lo = (odd_hi, odd_lo) if layer in (1, 4) else (even_hi, even_lo)
            return hi[:, m * n:(m + 1) * n], lo[:, m * n:(m + 1) * n]

        def result_full(i):
            g = groups[i]
            if g["layer"] == 2:
                return bottom_full[:, :]
            if g["layer"] == 6:
                return last_x[:, g["m"], :]
            n = B if g["half"] is None else HALF
            return full[:, split_groups(i) % 2, 0:n]

        def operands(g, k):
            layer, half = g["layer"], g["half"]
            if layer == 0:
                return x_hi[:, :], x_lo[:, :]
            if layer == 3:
                c = slice(half * HALF, (half + 1) * HALF)
                if k == 0:
                    return bottom_hi[:, c], bottom_lo[:, c]
                return pairs_hi[:, k - 1, :], pairs_lo[:, k - 1, :]
            n = B if half is None else HALF
            hi, lo = (odd_hi, odd_lo) if layer in (2, 5) else (even_hi, even_lo)
            return hi[:, k * n:(k + 1) * n], lo[:, k * n:(k + 1) * n]

        def piece_source(p):
            if p["kind"] == "bottom":
                return raw_bottom[0:p["parts"], p["at"]:p["at"] + p["size"]]
            return raw[p["layer"] - 3][:, p["at"]:p["at"] + p["size"]]

        def piece_loaded(eng, p):
            if p["kind"] == "bottom":
                eng.wait_ge(bottom_loaded[p["layer"]], 16)
            else:
                eng.wait_ge(top_loaded[p["layer"] - 3], 16)

        def schedule(bottom, tile, layer):
            bottom()
            tile(0)
            tile(1)
            for half in range(HALVES):
                layer(half, 3)
                layer(half, 4)
                if half == 0:
                    tile(2)
                layer(half, 5)
                layer(half, 6)
                layer(half, 7)
                if half == 0:
                    tile(3)

        block = ctx.enter_context(nc.Block())

        @block.sync
        def _(sp):
            sp.dma_start(cat_i[:, :], cat).then_inc(cat_loaded, 16)
            sp.wait_ge(zeroed, 1)
            sp.dma_start(x_dense[0:NUM_DENSE, :], dense).then_inc(dense_loaded, 16)
            for n, p in enumerate(pieces[:len(BOTTOM)]):
                sp.dma_start(piece_source(p), bottom_w[0:p["parts"], p["at"]:p["at"] + p["size"]])\
                  .then_inc(bottom_loaded[n], 16)
            sp.dma_start(bias[:, :], biases).then_inc(bias_loaded, 16)
            sp.dma_start(ident[:, :], identity).then_inc(ident_loaded, 16)
            sp.dma_start(mask[:, :, :], b_mask).then_inc(mask_loaded, 16)
            for n in range(len(TOP)):
                sp.dma_start(raw[n][:, :], top_w[n]).then_inc(top_loaded[n], 16)
            sp.dma_start(raw_last[:, :], last_w).then_inc(last_loaded, 16)
            sp.dma_start(bias_last[:, :], last_bias).then_inc(bias_last_loaded, 16)
            sp.wait_ge(taken, len(groups))
            sp.dma_start(out, logits[:, :]).then_inc(stored, 16)
            sp.wait_ge(stored, 16)

        @block.gpsimd
        def _(pool):
            nc.gpsimd.iota(table_base[:, :].rearrange("p (b t) -> p b t", b=TILES),
                           pattern=[[0, TILES], [V, T]], base=0, channel_multiplier=0).then_inc(base_ready, 1)
            pool.wait_ge(index_step, 6)
            for b in range(TILES):
                for j in range(BANKS):
                    if b == 1 and max(bank_tables(j)) >= T - bottom_slots:
                        pool.wait_ge(w_hi_ready, len(BOTTOM))
                        pool.wait_ge(w_lo_ready, len(BOTTOM))
                    if b >= 2:
                        pool.wait_ge(bank_turned, (b - 2) * BANKS + j + 1)
                    for t in bank_tables(j):
                        c = b * T + t
                        pool.indirect_dma_start(
                            rows[:, (b % 2) * T + t, :], None, emb,
                            bass.IndirectOffsetOnAxis(ap=row_index[:, c:c + 1], axis=0),
                        ).then_inc(gathered[b * BANKS + j], 16)

        @block.tensor
        def _(pe):
            def product(i):
                g = groups[i]
                p = pieces[g["piece"]]
                slot = g["piece"] % W_RING
                kt = p["size"] // P if g["half"] is not None else BOTTOM[g["layer"]][0]
                parts = p["parts"]
                n = B if g["half"] is None else HALF
                base = g["m"] * kt * P if g["half"] is None else 0
                pe.wait_ge(w_hi_ready, g["piece"] + 1)
                pe.wait_ge(w_lo_ready, g["piece"] + 1)
                if i >= 2:
                    pe.wait_ge(taken, i - 1)
                last = None
                for k in range(kt):
                    hi, lo = operands(g, k)
                    wh = w_hi[0:parts, slot, base + k * P:base + (k + 1) * P]
                    wl = w_lo[0:parts, slot, base + k * P:base + (k + 1) * P]
                    first_k = k == 0
                    if g["m"] == 0 and g["layer"] in (1, 2, 4, 5, 6):
                        source = i - kt + k
                        pe.wait_ge(taken, source + 1)
                    pe.matmul(acc[:, i % 2, 0:n], wh, hi, start=first_k, stop=False)
                    pe.matmul(acc[:, i % 2, 0:n], wl, hi, start=False, stop=False)
                    if g["m"] == 0 and g["layer"] in (1, 2, 4, 5, 6):
                        pe.wait_ge(lo_ready, split_groups(source + 1))
                    last = pe.matmul(acc[:, i % 2, 0:n], wh, lo, start=False, stop=k == kt - 1)
                last.then_inc(group_done, 1)

            def bottom():
                pe.wait_ge(x_hi_ready, 1)
                pe.wait_ge(x_lo_ready, 1)
                for i in range(n_bottom):
                    product(i)

            def layer(half, n):
                ids = group_range(half, n)
                if n == 3:
                    pe.wait_ge(taken, n_bottom)
                    pe.wait_ge(lo_ready, n_bottom)
                    pe.wait_ge(pairs_hi_ready, 2 * half + 2)
                    pe.wait_ge(pairs_lo_ready, 2 * half + 2)
                if n < 7:
                    for i in ids:
                        product(i)
                    return
                i = ids[0]
                pe.wait_ge(last_loaded, 16)
                pe.wait_ge(taken, i)
                for k in range(2):
                    mm = pe.matmul(acc[0:1, i % 2, 0:HALF], raw_last[:, k:k + 1], last_x[:, k, :],
                                   start=k == 0, stop=k == 1)
                mm.then_inc(group_done, 1)

            def tile(b):
                if b == 0:
                    pe.wait_ge(ident_loaded, 16)
                for j in range(BANKS):
                    u = b * BANKS + j
                    pe.wait_ge(gathered[u], 16 * len(bank_tables(j)))
                    if u >= 2:
                        if u % 2 == 0:
                            pe.wait_ge(even_moved, u // 2)
                        else:
                            pe.wait_ge(odd_moved, u // 2)
                    for t in bank_tables(j):
                        tr = pe.transpose(turned[:, u % 2, t % BANK_TABLES, :], rows[:, (b % 2) * T + t, :],
                                          ident[:, :])
                    tr.then_inc(bank_turned, 1)
                done = (b + 1) * BANKS
                pe.wait_ge(even_moved, (done + 1) // 2)
                pe.wait_ge(odd_moved, done // 2)
                pe.wait_ge(first_moved, b + 1)
                for c in range(CHUNKS):
                    n = b * CHUNKS + c
                    if n >= 2:
                        pe.wait_ge(b_moved, n - 1)
                    for i in range(CHUNK):
                        g = c * CHUNK + i
                        mm = pe.matmul(dots[:, n % 2, i, 0:GROUP * NF],
                                       feats[:, g, :, :].rearrange("p s f -> p (s f)"), feats[:, g, :, 0:NF],
                                       start=True, stop=True)
                    mm.then_inc(chunk_done, 1)

            schedule(bottom, tile, layer)

        @block.scalar
        def _(act):
            def split_piece(n):
                if n >= len(pieces):
                    return
                p = pieces[n]
                piece_loaded(act, p)
                if n >= W_RING:
                    act.wait_ge(group_done, last_group_of_piece[n - W_RING] + 1)
                    act.wait_ge(w_lo_ready, n - W_RING + 1)
                nc.scalar.copy(w_hi[0:p["parts"], n % W_RING, 0:p["size"]], piece_source(p)).then_inc(w_hi_ready, 1)

            def take(i):
                g = groups[i]
                act.wait_ge(group_done, i + 1)
                if g["layer"] == 7:
                    act.wait_ge(bias_last_loaded, 16)
                    nc.scalar.activation(logits[:, g["half"] * HALF:(g["half"] + 1) * HALF], acc[0:1, i % 2, 0:HALF],
                                         ACT.Identity, bias=bias_last[:, 0:1]).then_inc(taken, 1)
                    return
                n = B if g["half"] is None else HALF
                col = BIAS_COLS[g["layer"]] + g["m"]
                if g["split"]:
                    s = split_groups(i)
                    if s >= 2:
                        act.wait_ge(lo_ready, s - 1)
                    hi, _ = result_hi_lo(g)
                    nc.scalar.activation(hi, acc[:, i % 2, 0:n], ACT.Relu, bias=bias[:, col:col + 1])
                nc.scalar.activation(result_full(i), acc[:, i % 2, 0:n], ACT.Relu, bias=bias[:, col:col + 1])\
                  .then_inc(taken, 1)

            def bottom():
                act.wait_ge(dense_loaded, 16)
                act.wait_ge(zeroed, 1)
                nc.scalar.copy(x_hi[:, :], x_dense[:, :]).then_inc(x_hi_ready, 1)
                for n in range(W_AHEAD):
                    split_piece(n)
                act.wait_ge(bias_loaded, 16)
                for i in range(n_bottom):
                    take(i)
                for n in range(W_AHEAD, len(BOTTOM) + W_AHEAD):
                    split_piece(n)

            def layer(half, n):
                for i in group_range(half, n):
                    if groups[i]["piece"] is not None:
                        split_piece(groups[i]["piece"] + W_AHEAD)
                    take(i)

            def tile(b):
                for j in range(BANKS):
                    u = b * BANKS + j
                    if u % 2 == 0:
                        if j < 2 and b > 0:
                            act.wait_ge(chunk_done, b * CHUNKS)
                        act.wait_ge(bank_turned, u + 1)
                        w = len(bank_tables(j))
                        f = 1 + j * BANK_TABLES
                        nc.scalar.copy(feats[:, :, :, f:f + w].rearrange("d i s n -> d n s i"),
                                       turned[:, u % 2, 0:w, :].rearrange("d n (s i) -> d n s i", s=GROUP)).then_inc(even_moved, 1)
                if b == 0:
                    act.wait_ge(zeroed, 3)
                if b >= 2:
                    act.wait_ge(pairs_lo_ready, b - 1)
                for c in range(CHUNKS):
                    n = b * CHUNKS + c
                    act.wait_ge(chunk_done, n + 1)
                    for s in range(GROUP):
                        block_cols = s * NF
                        src = dots[QUAD * s:QUAD * s + NF, n % 2, :, :].rearrange("p i c -> p c i")
                        at = s * QUAD + c * CHUNK
                        for q in range(3):
                            nc.scalar.copy(pairs[QUAD * q:QUAD * q + NF, b % 2, :, at:at + CHUNK],
                                           src[:, block_cols + q * KT:block_cols + (q + 1) * KT, :])
                        nc.scalar.copy(pairs[QUAD * 3:QUAD * 3 + NF, b % 2, 0, at:at + CHUNK],
                                       src[:, block_cols + 3 * KT, :])
                        last = nc.scalar.copy(pairs[QUAD * 3:QUAD * 3 + WIN, b % 2, 1, at:at + CHUNK],
                                              src[0:WIN, block_cols + NF - 1, :])
                    last.then_inc(a_moved, 1)
                act.wait_ge(b_moved, (b + 1) * CHUNKS)
                c0 = (b % 2) * TILE
                nc.scalar.copy(pairs_hi[:, :, c0:c0 + TILE], pairs[:, b % 2, :, :]).then_inc(pairs_hi_ready, 1)

            schedule(bottom, tile, layer)

        @block.vector
        def _(dve):
            def lo_piece(n):
                if n >= len(pieces):
                    return
                p = pieces[n]
                a = slice(0, p["parts"])
                if n >= W_RING:
                    dve.wait_ge(group_done, last_group_of_piece[n - W_RING] + 1)
                dve.wait_ge(w_hi_ready, n + 1)
                nc.vector.tensor_tensor(w_lo[a, n % W_RING, 0:p["size"]], piece_source(p),
                                        w_hi[a, n % W_RING, 0:p["size"]].bitcast(F32), ALU.subtract)\
                  .then_inc(w_lo_ready, 1)

            def lo_result(i):
                g = groups[i]
                if not g["split"]:
                    return
                hi, lo = result_hi_lo(g)
                dve.wait_ge(taken, i + 1)
                nc.vector.tensor_tensor(lo, result_full(i), hi.bitcast(F32), ALU.subtract).then_inc(lo_ready, 1)

            def indices():
                dve.wait_ge(cat_loaded, 16)
                nc.vector.tensor_copy(cat_f[:, :], cat_i[:, :]).then_inc(index_step, 1)
                dve.wait_ge(index_step, 1)
                nc.vector.tensor_scalar(wrap[:, :], cat_f[:, :], 0.0, float(V), ALU.is_lt, ALU.mult).then_inc(index_step, 1)
                dve.wait_ge(index_step, 2)
                nc.vector.tensor_tensor(row_f[:, :], cat_f[:, :], wrap[:, :], ALU.add).then_inc(index_step, 1)
                dve.wait_ge(index_step, 3)
                nc.vector.tensor_scalar(cat_f[:, :], row_f[:, :], 0.0, float(V - 1), ALU.max, ALU.min).then_inc(index_step, 1)
                dve.wait_ge(base_ready, 1)
                nc.vector.tensor_copy(wrap[:, :], table_base[:, :]).then_inc(index_step, 1)
                dve.wait_ge(index_step, 5)
                nc.vector.tensor_tensor(row_index[:, :], cat_f[:, :], wrap[:, :], ALU.add).then_inc(index_step, 1)

            def bottom():
                nc.vector.memset(x_dense[:, :], 0.0).then_inc(zeroed, 1)
                indices()
                nc.vector.memset(feats[:, :, :, NF:QUAD], 0.0).then_inc(zeroed, 1)
                nc.vector.memset(pairs[:, :, :, :], 0.0).then_inc(zeroed, 1)
                dve.wait_ge(x_hi_ready, 1)
                nc.vector.tensor_tensor(x_lo[:, :], x_dense[:, :], x_hi[:, :].bitcast(F32), ALU.subtract)\
                  .then_inc(x_lo_ready, 1)
                for n in range(W_AHEAD):
                    lo_piece(n)
                for i in range(n_bottom):
                    lo_result(i)
                for n in range(W_AHEAD, len(BOTTOM) + W_AHEAD):
                    lo_piece(n)

            def layer(half, n):
                for i in group_range(half, n):
                    if groups[i]["piece"] is not None:
                        lo_piece(groups[i]["piece"] + W_AHEAD)
                    lo_result(i)

            def tile(b):
                if b == 0:
                    dve.wait_ge(mask_loaded, 16)
                if b > 0:
                    dve.wait_ge(chunk_done, b * CHUNKS)
                dve.wait_ge(taken, n_bottom)
                nc.vector.tensor_copy(feats[:, :, :, 0].rearrange("d i s -> d s i"),
                                      bottom_full[:, b * TILE:(b + 1) * TILE].rearrange("d (s i) -> d s i", s=GROUP)).then_inc(first_moved, 1)
                for j in range(BANKS):
                    u = b * BANKS + j
                    if u % 2 == 1:
                        dve.wait_ge(bank_turned, u + 1)
                        w = len(bank_tables(j))
                        f = 1 + j * BANK_TABLES
                        nc.vector.tensor_copy(feats[:, :, :, f:f + w].rearrange("d i s n -> d n s i"),
                                              turned[:, u % 2, 0:w, :].rearrange("d n (s i) -> d n s i", s=GROUP)).then_inc(odd_moved, 1)
                for c in range(CHUNKS):
                    n = b * CHUNKS + c
                    dve.wait_ge(a_moved, n + 1)
                    for s in range(GROUP):
                        src = dots[QUAD * s:QUAD * s + NF, n % 2, :, :].rearrange("p i c -> p c i")
                        at = s * QUAD + c * CHUNK
                        for q in range(GROUP):
                            w = min(KT, WIN - q * KT)
                            col = s * NF + WIN + q * KT
                            last = nc.vector.copy_predicated(
                                pairs[QUAD * q:QUAD * q + NF, b % 2, 0:w, at:at + CHUNK],
                                mask[QUAD * q:QUAD * q + NF, q * KT:q * KT + w, :],
                                src[:, col:col + w, :])
                    last.then_inc(b_moved, 1)
                dve.wait_ge(pairs_hi_ready, b + 1)
                c0 = (b % 2) * TILE
                nc.vector.tensor_tensor(pairs_lo[:, :, c0:c0 + TILE], pairs[:, b % 2, :, :],
                                        pairs_hi[:, :, c0:c0 + TILE].bitcast(F32), ALU.subtract)\
                  .then_inc(pairs_lo_ready, 1)

            schedule(bottom, tile, layer)


def first_top_rows():
    rows = np.full((1 + KT, P), -1)
    rows[0] = np.arange(E)
    pair = {}
    for at, (i, j) in enumerate(zip(*np.triu_indices(NF, k=1))):
        pair[i, j] = pair[j, i] = E + at
    for k in range(SLOTS):
        for r in range(NF):
            if k == WIN:
                c = NF - 1 if r < WIN else r
            else:
                c = k if k < r <= k + WIN else k + WIN
                if r == k:
                    c = r
            if c != r:
                rows[1 + k % KT, QUAD * (k // KT) + r] = pair[r, c]
    rows[1, NF] = TOP_PAD - 1
    assert sorted(rows[rows >= 0]) == list(range(TOP_PAD))
    return rows


def by_output_tile(w, kt):
    n = w.shape[1]
    return np.ascontiguousarray(w.reshape(kt, P, n // P, P).transpose(1, 2, 0, 3).reshape(P, -1))


def kernel(**inputs):
    import concourse.bacc as bacc
    from concourse.bass_utils import run_bass_kernel_spmd

    a = {k.replace("L0_rec_", ""): np.asarray(v) for k, v in inputs.items()}
    nc = bacc.Bacc("TRN2", target_bir_lowering=False, num_devices=1)
    arrays = {}

    def dram(name, x):
        arrays[name] = np.ascontiguousarray(x)
        return nc.dram_tensor(name, x.shape, mybir.dt.from_np(x.dtype), kind="ExternalInput").ap()

    bw0 = np.zeros((P, BOTTOM[0][1] * P), np.float32)
    bw0[0:PAD_DENSE] = a["bw0"]
    bottom_w = np.concatenate([bw0, by_output_tile(a["bw1"], 4), by_output_tile(a["bw2"], 2)], axis=1)
    rows = first_top_rows()
    tw0 = np.zeros(((1 + KT) * P, a["tw0"].shape[1]), np.float32)
    tw0[rows.ravel() >= 0] = a["tw0"][rows.ravel()[rows.ravel() >= 0]]
    tops = [tw0] + [a[f"tw{n}"] for n in (1, 2, 3)]
    biases = np.concatenate([a[k].reshape(-1, P).T for k in ("bb0", "bb1", "bb2", "tb0", "tb1", "tb2", "tb3")], axis=1)
    b_mask = np.ones((P, WIN, CHUNK), np.uint32)
    for q in range(P // QUAD):
        for k in range(WIN):
            b_mask[QUAD * q + k + 1:QUAD * q + k + 1 + WIN, k] = 0
    args = [
        dram("cat", a["r_cat_features"].reshape(TILES, TILE, T).transpose(1, 0, 2).reshape(TILE, TILES * T)),
        dram("dense", a["r_numerical"].T),
        dram("emb", a["emb_tables"].reshape(T * V, E)),
        dram("bottom_w", bottom_w),
        [dram(f"top_w{n}", by_output_tile(w, TOP[n][0])) for n, w in enumerate(tops)],
        dram("last_w", a["tw4"].reshape(2, P).T),
        dram("biases", biases),
        dram("last_bias", a["tb4"].reshape(1, 1)),
        dram("identity", np.eye(P, dtype=np.float32)),
        dram("b_mask", b_mask),
    ]
    out = nc.dram_tensor("out", (B, 1), F32, kind="ExternalOutput").ap()
    dlrm(nc, *args, out.rearrange("b o -> o b"))
    r = run_bass_kernel_spmd(nc, [arrays], core_ids=[0])
    return r.results[0]["out"]
```

```python
from contextlib import ExitStack

import concourse.bass as bass
import numpy as np
from concourse import mybir

F32 = mybir.dt.float32
F32R = mybir.dt.float32r
I32 = mybir.dt.int32
U32 = mybir.dt.uint32
ALU = mybir.AluOpType
ACT = mybir.ActivationFunctionType

P = 128
B = 512
E = 128
T = 26
V = 12500
NF = T + 1
NUM_DENSE, PAD_DENSE = 13, 16
TILE = 128
TILES = B // TILE
HALF = 256
HALVES = B // HALF
TOP_PAD = 480

QUAD = 32
WIN = NF // 2
SLOTS = WIN + 1
KT = 4

BOTTOM = [(1, 4), (4, 2), (2, 1), (2, KT)]
TOP = [(KT, 8), (8, 8), (8, 4), (4, 2)]
LAYERS = BOTTOM + TOP + [(2, 1)]
TOP0, TOP1, TOP2, TOP3, LAST = range(len(BOTTOM), len(LAYERS))
BIAS_COLS = [sum(mt for _, mt in LAYERS[:n]) for n in range(len(LAYERS))]

BANK_TABLES = 4
BANKS = -(-T // BANK_TABLES)
GROUP = P // QUAD
CHUNK = 8
CHUNKS = TILE // (GROUP * CHUNK)

W_RING = 4
W_AHEAD = W_RING - 1
PIECE = 1024

LOADS = [(0, m, 2) for m in range(0, 8, 2)] + [(1, m, 1) for m in range(8)] + [(2, m, 1) for m in range(4)] + [(3, 0, 2)]


def bank_tables(bank):
    return range(bank * BANK_TABLES, min(T, (bank + 1) * BANK_TABLES))


def order():
    groups, pieces, work = [], [], []

    def group(layer, m, at, n, split):
        piece = None
        if split:
            piece = len(pieces)
            pieces.append(dict(layer=layer, m=m, group=len(groups)))
        groups.append(dict(layer=layer, m=m, at=at, n=n, piece=piece,
                           split_result=layer in (TOP1, TOP2) or (layer == TOP0 and at >= HALF)))
        return ("group", len(groups) - 1)

    def layer(n, at, cols, split=False):
        return [group(n, m, at, cols, split) for m in range(LAYERS[n][1])]

    def banks(b):
        return [("bank", b * BANKS + j) for j in range(BANKS)]

    def chunks(b):
        return [("chunk", b * CHUNKS + c) for c in range(CHUNKS)]

    def between(main, side, places):
        out = []
        for at, x in enumerate(main):
            out += [y for y, p in zip(side, places) if p == at] + [x]
        return out + [y for y, p in zip(side, places) if p >= len(main)]

    def solo(tile):
        return layer(TOP0, tile * TILE, TILE) + layer(TOP1, tile * TILE, TILE)

    main = [x for n in range(len(BOTTOM)) for x in layer(n, 0, B)]
    work += between(main, banks(0)[0:5], BETWEEN_BOTTOM)
    work += [("first", 0)] + banks(0)[5:] + chunks(0)
    work += between(solo(0), [("first", 1)] + banks(1) + chunks(1), BETWEEN_TILE0)
    work += between(solo(1), [("pieces",), ("first", 2)] + banks(2) + chunks(2)[0:2], BETWEEN_TILE1)
    main = layer(TOP2, 0, HALF, True) + layer(TOP0, 2 * TILE, TILE) + layer(TOP3, 0, HALF, True) + layer(LAST, 0, HALF)
    work += between(main, chunks(2)[2:] + [("first", 3)] + banks(3) + chunks(3), BETWEEN_HALF0)
    work += layer(TOP0, 3 * TILE, TILE)
    for n in (TOP1, TOP2, TOP3):
        work += layer(n, HALF, HALF, True)
    work += layer(LAST, HALF, HALF)
    return groups, pieces, work


BETWEEN_BOTTOM = [4, 5, 6, 9, 11]
BETWEEN_TILE0 = [0] + [0, 0, 5, 9, 11, 12, 13] + [14, 15, 15, 15]
BETWEEN_TILE1 = [2, 0] + [0, 0, 3, 6, 9, 12, 13] + [15, 16]
BETWEEN_HALF0 = [1, 2, 3] + [3, 3, 4, 5, 6, 7, 8] + [9, 11, 13, 14]


def dlrm(nc, cat, dense, emb, bottom_w, top_w, last_w, biases, last_bias, identity, b_mask, out):
    groups, pieces, work = order()
    n_bottom = sum(mt for _, mt in BOTTOM)

    def split_results(i):
        return sum(g["split_result"] for g in groups[:i])

    def writer(g, k, i):
        source = 1 if g["layer"] == 3 else g["layer"] - 1
        return max(n for n in range(i) if groups[n]["layer"] == source and groups[n]["m"] == k)

    ctx = ExitStack()
    with ctx:
        def sb(name, shape, dt=F32):
            return ctx.enter_context(nc.sbuf_tensor(name, shape, dt))

        def sem(name):
            return ctx.enter_context(nc.semaphore(name))

        cat_i = sb("cat_i", [P, TILES * T], I32)
        wrap = sb("wrap", [P, TILES * T])
        row_f = sb("row_f", [P, TILES * T])
        row_c = sb("row_c", [P, TILES * T])
        table_base = sb("table_base", [P, TILES * T], I32)
        row_index = sb("row_index", [P, TILES * T], U32)
        rows = sb("rows", [P, 2 * T, E])
        ident = sb("ident", [P, P])
        mask = sb("mask", [P, WIN, CHUNK], U32)
        bias = sb("bias", [P, BIAS_COLS[LAST]])
        bias_last = sb("bias_last", [1, 1])
        feats = sb("feats", [P, QUAD, GROUP, QUAD])
        bottom_full = sb("bottom_full", [P, B])
        x_dense = bottom_full[0:PAD_DENSE, :]
        pairs = sb("pairs", [P, KT, B])
        plain = sb("plain", [P, 8 * TILE])
        logits = plain[0:1, 0:B]
        split_of = {n: [sb(f"top{n - TOP0}_{part}", [P, LAYERS[n][1] * HALF], F32R) for part in ("hi", "lo")]
                    for n in (TOP0, TOP1, TOP2)}
        full = sb("full", [P, 2, HALF])
        last_x = sb("last_x", [P, 2, HALF])
        raw = [sb(f"raw{n}", [P, mt * kt * P]) for n, (kt, mt) in enumerate(TOP)]
        raw_last = sb("raw_last", [P, 2])
        w_hi = sb("w_hi", [P, W_RING, PIECE], F32R)
        w_lo = sb("w_lo", [P, W_RING, PIECE], F32R)

        bottom_at = [sum(kt * mt * P for kt, mt in BOTTOM[:n]) for n in range(len(BOTTOM) + 1)]
        bottom_slots = bottom_at[-1] // E
        raw_bottom = rows[:, 2 * T - bottom_slots:2 * T, :].rearrange("p t e -> p (t e)")

        turned = ctx.enter_context(nc.psum_tensor("turned", [P, 2, BANK_TABLES, TILE], F32))
        dots = ctx.enter_context(nc.psum_tensor("dots", [P, 2, CHUNK, P], F32))
        acc = ctx.enter_context(nc.psum_tensor("acc", [P, 2, B], F32))

        cat_loaded, dense_loaded, bias_loaded = sem("cat_loaded"), sem("dense_loaded"), sem("bias_loaded")
        ident_loaded, mask_loaded = sem("ident_loaded"), sem("mask_loaded")
        bottom_loaded = [sem(f"bottom{n}_loaded") for n in range(len(BOTTOM))]
        top_loaded = [sem(f"top{n}_{m}_loaded") for n, m, _ in LOADS]
        last_loaded, bias_last_loaded = sem("last_loaded"), sem("bias_last_loaded")
        gathered = [sem(f"gathered{u}") for u in range(TILES * BANKS)]
        stored = sem("stored")
        base_ready = sem("base_ready")
        index_step = sem("index_step")
        zeroed = sem("zeroed")
        w_hi_ready, w_lo_ready = sem("w_hi_ready"), sem("w_lo_ready")
        group_done = sem("group_done")
        taken = sem("taken")
        lo_ready = sem("lo_ready")
        bank_turned = sem("bank_turned")
        even_moved, odd_moved = sem("even_moved"), sem("odd_moved")
        first_moved = sem("first_moved")
        chunk_done = sem("chunk_done")
        a_moved = sem("a_moved")
        b_moved = sem("b_moved")

        def result(i):
            g = groups[i]
            layer, m, at, n = g["layer"], g["m"], g["at"], g["n"]
            if g["split_result"]:
                return full[:, split_results(i) % 2, 0:n]
            if layer == 2:
                return bottom_full[:, :]
            if layer in (0, 3):
                return pairs[:, m, :]
            if layer in (1, TOP0):
                return plain[:, m * n:(m + 1) * n]
            assert layer == TOP3
            return last_x[:, m, :]

        def split_result(g):
            hi, lo = split_of[g["layer"]]
            c = g["m"] * HALF + g["at"] % HALF
            return hi[:, c:c + g["n"]], lo[:, c:c + g["n"]]

        def plain_x(g, k):
            layer, at, n = g["layer"], g["at"], g["n"]
            if layer == 0:
                return x_dense
            if layer in (1, TOP0):
                return pairs[:, k, at:at + n]
            if layer == LAST:
                return last_x[:, k, :]
            return plain[:, k * n:(k + 1) * n]

        def split_x(g, k):
            hi, lo = split_of[g["layer"] - 1]
            return hi[:, k * HALF:(k + 1) * HALF], lo[:, k * HALF:(k + 1) * HALF]

        def weights(layer, m):
            kt = LAYERS[layer][0]
            if layer < len(BOTTOM):
                at = bottom_at[layer] + m * kt * P
                return raw_bottom[0:PAD_DENSE if layer == 0 else P, at:at + kt * P]
            if layer == LAST:
                return raw_last[:, :]
            return raw[layer - TOP0][:, m * kt * P:(m + 1) * kt * P]

        def weights_loaded(eng, layer, m):
            if layer < len(BOTTOM):
                eng.wait_ge(bottom_loaded[layer], 16)
            elif layer == LAST:
                eng.wait_ge(last_loaded, 16)
            else:
                load = next(x for x, (n, first, count) in enumerate(LOADS)
                            if n == layer - TOP0 and first <= m < first + count)
                eng.wait_ge(top_loaded[load], 16)

        block = ctx.enter_context(nc.Block())

        @block.sync
        def _(sp):
            sp.dma_start(cat_i[:, :], cat).then_inc(cat_loaded, 16)
            sp.wait_ge(zeroed, 1)
            sp.dma_start(x_dense[0:NUM_DENSE, :], dense).then_inc(dense_loaded, 16)
            for n in range(len(BOTTOM)):
                parts = PAD_DENSE if n == 0 else P
                c = slice(bottom_at[n], bottom_at[n + 1])
                sp.dma_start(raw_bottom[0:parts, c], bottom_w[0:parts, c]).then_inc(bottom_loaded[n], 16)
                if n == 0:
                    sp.dma_start(bias[:, :], biases).then_inc(bias_loaded, 16)
            sp.dma_start(ident[:, :], identity).then_inc(ident_loaded, 16)
            sp.dma_start(mask[:, :, :], b_mask).then_inc(mask_loaded, 16)
            for x, (n, m, count) in enumerate(LOADS):
                if x >= 2:
                    sp.wait_ge(gathered[x - 2], 16 * len(bank_tables((x - 2) % BANKS)))
                size = TOP[n][0] * P
                c = slice(m * size, (m + count) * size)
                sp.dma_start(raw[n][:, c], top_w[n][:, c]).then_inc(top_loaded[x], 16)
            sp.dma_start(raw_last[:, :], last_w).then_inc(last_loaded, 16)
            sp.dma_start(bias_last[:, :], last_bias).then_inc(bias_last_loaded, 16)
            sp.wait_ge(taken, len(groups))
            sp.dma_start(out, logits).then_inc(stored, 16)
            sp.wait_ge(stored, 16)

        @block.gpsimd
        def _(pool):
            nc.gpsimd.iota(table_base[:, :].rearrange("p (b t) -> p b t", b=TILES),
                           pattern=[[0, TILES], [V, T]], base=0, channel_multiplier=0).then_inc(base_ready, 1)
            pool.wait_ge(index_step, 4)
            for b in range(TILES):
                for j in range(BANKS):
                    if b == 1 and max(bank_tables(j)) >= T - bottom_slots:
                        pool.wait_ge(group_done, n_bottom)
                    if b >= 2:
                        pool.wait_ge(bank_turned, (b - 2) * BANKS + j + 1)
                    for t in bank_tables(j):
                        c = b * T + t
                        pool.indirect_dma_start(
                            rows[:, (b % 2) * T + t, :], None, emb,
                            bass.IndirectOffsetOnAxis(ap=row_index[:, c:c + 1], axis=0),
                        ).then_inc(gathered[b * BANKS + j], 16)

        @block.tensor
        def _(pe):
            def plain_group(i):
                g = groups[i]
                kt = LAYERS[g["layer"]][0]
                w = weights(g["layer"], g["m"])
                cols = P if g["layer"] < LAST else 1
                weights_loaded(pe, g["layer"], g["m"])
                if g["layer"] == 0:
                    pe.wait_ge(dense_loaded, 16)
                if i >= 2:
                    pe.wait_ge(taken, i - 1)
                if g["layer"] == TOP0:
                    pe.wait_ge(b_moved, (g["at"] // TILE + 1) * CHUNKS)
                for k in range(kt):
                    if g["m"] == 0 and g["layer"] not in (0, TOP0):
                        pe.wait_ge(taken, writer(g, k, i) + 1)
                    mm = pe.matmul(acc[0:cols, i % 2, 0:g["n"]], w[:, k * cols:(k + 1) * cols], plain_x(g, k),
                                   start=k == 0, stop=k == kt - 1)
                mm.then_inc(group_done, 1)

            def split_group(i):
                g = groups[i]
                kt = LAYERS[g["layer"]][0]
                slot = g["piece"] % W_RING
                pe.wait_ge(w_hi_ready, g["piece"] + 1)
                pe.wait_ge(w_lo_ready, g["piece"] + 1)
                pe.wait_ge(taken, i - 1)
                for k in range(kt):
                    hi, lo = split_x(g, k)
                    wh = w_hi[:, slot, k * P:(k + 1) * P]
                    wl = w_lo[:, slot, k * P:(k + 1) * P]
                    if g["m"] == 0:
                        pe.wait_ge(taken, writer(g, k, i) + 1)
                    pe.matmul(acc[:, i % 2, 0:HALF], wh, hi, start=k == 0, stop=False)
                    pe.matmul(acc[:, i % 2, 0:HALF], wl, hi, start=False, stop=False)
                    if g["m"] == 0:
                        pe.wait_ge(lo_ready, split_results(writer(g, k, i) + 1))
                    mm = pe.matmul(acc[:, i % 2, 0:HALF], wh, lo, start=False, stop=k == kt - 1)
                mm.then_inc(group_done, 1)

            def bank(u):
                b, j = divmod(u, BANKS)
                pe.wait_ge(gathered[u], 16 * len(bank_tables(j)))
                if u == 0:
                    pe.wait_ge(ident_loaded, 16)
                if u >= 2:
                    pe.wait_ge(odd_moved if u % 2 else even_moved, u // 2)
                for t in bank_tables(j):
                    tr = pe.transpose(turned[:, u % 2, t % BANK_TABLES, :], rows[:, (b % 2) * T + t, :], ident[:, :])
                tr.then_inc(bank_turned, 1)

            def chunk(n):
                b, c = divmod(n, CHUNKS)
                if c == 0:
                    done = (b + 1) * BANKS
                    pe.wait_ge(even_moved, (done + 1) // 2)
                    pe.wait_ge(odd_moved, done // 2)
                    pe.wait_ge(first_moved, b + 1)
                if n >= 2:
                    pe.wait_ge(b_moved, n - 1)
                for x in range(CHUNK):
                    i = c * CHUNK + x
                    mm = pe.matmul(dots[:, n % 2, x, 0:GROUP * NF],
                                   feats[:, i, :, :].rearrange("p s f -> p (s f)"), feats[:, i, :, 0:NF],
                                   start=True, stop=True)
                mm.then_inc(chunk_done, 1)

            for what, *n in work:
                if what == "group" and groups[n[0]]["piece"] is None:
                    plain_group(*n)
                elif what == "group":
                    split_group(*n)
                elif what == "bank":
                    bank(*n)
                elif what == "chunk":
                    chunk(*n)

        @block.scalar
        def _(act):
            def split_piece(n):
                if n >= len(pieces):
                    return
                p = pieces[n]
                size = LAYERS[p["layer"]][0] * P
                weights_loaded(act, p["layer"], p["m"])
                if n >= W_RING:
                    act.wait_ge(group_done, pieces[n - W_RING]["group"] + 1)
                    act.wait_ge(w_lo_ready, n - W_RING + 1)
                nc.scalar.copy(w_hi[:, n % W_RING, 0:size], weights(p["layer"], p["m"])).then_inc(w_hi_ready, 1)

            def take(i):
                g = groups[i]
                n = g["n"]
                if g["piece"] is not None:
                    split_piece(g["piece"] + W_AHEAD)
                act.wait_ge(group_done, i + 1)
                if g["layer"] == LAST:
                    act.wait_ge(bias_last_loaded, 16)
                    nc.scalar.activation(logits[:, g["at"]:g["at"] + n], acc[0:1, i % 2, 0:n],
                                         ACT.Identity, bias=bias_last[:, 0:1]).then_inc(taken, 1)
                    return
                if i == 0:
                    act.wait_ge(bias_loaded, 16)
                col = BIAS_COLS[g["layer"]] + g["m"]
                if g["split_result"]:
                    if split_results(i) >= 2:
                        act.wait_ge(lo_ready, split_results(i) - 1)
                    nc.scalar.activation(split_result(g)[0], acc[:, i % 2, 0:n], ACT.Relu, bias=bias[:, col:col + 1])
                nc.scalar.activation(result(i), acc[:, i % 2, 0:n], ACT.Relu, bias=bias[:, col:col + 1])\
                  .then_inc(taken, 1)

            def move_bank(u):
                b, j = divmod(u, BANKS)
                if u % 2:
                    return
                if b > 0:
                    act.wait_ge(chunk_done, b * CHUNKS)
                act.wait_ge(bank_turned, u + 1)
                if u == 0:
                    act.wait_ge(zeroed, 2)
                w = len(bank_tables(j))
                f = 1 + j * BANK_TABLES
                nc.scalar.copy(feats[:, :, :, f:f + w].rearrange("d i s n -> d n s i"),
                               turned[:, u % 2, 0:w, :].rearrange("d n (s i) -> d n s i", s=GROUP))\
                  .then_inc(even_moved, 1)

            def move_chunk(n):
                b, c = divmod(n, CHUNKS)
                act.wait_ge(chunk_done, n + 1)
                for s in range(GROUP):
                    src = dots[QUAD * s:QUAD * s + NF, n % 2, :, s * NF:(s + 1) * NF].rearrange("p i c -> p c i")
                    at = b * TILE + s * QUAD + c * CHUNK
                    for q in range(3):
                        nc.scalar.copy(pairs[QUAD * q:QUAD * q + NF, :, at:at + CHUNK], src[:, q * KT:(q + 1) * KT, :])
                    nc.scalar.copy(pairs[QUAD * 3:QUAD * 3 + NF, 0, at:at + CHUNK], src[:, 3 * KT, :])
                    nc.scalar.copy(pairs[QUAD * 3:QUAD * 3 + WIN, 1, at:at + CHUNK], src[0:WIN, NF - 1, :])\
                      .then_inc(a_moved, 1)

            for what, *n in work:
                if what == "group":
                    take(*n)
                elif what == "bank":
                    move_bank(*n)
                elif what == "chunk":
                    move_chunk(*n)
                elif what == "pieces":
                    for p in range(W_AHEAD):
                        split_piece(p)

        @block.vector
        def _(dve):
            def lo_piece(n):
                if n >= len(pieces):
                    return
                p = pieces[n]
                size = LAYERS[p["layer"]][0] * P
                if n >= W_RING:
                    dve.wait_ge(group_done, pieces[n - W_RING]["group"] + 1)
                dve.wait_ge(w_hi_ready, n + 1)
                nc.vector.tensor_tensor(w_lo[:, n % W_RING, 0:size], weights(p["layer"], p["m"]),
                                        w_hi[:, n % W_RING, 0:size].bitcast(F32), ALU.subtract)\
                  .then_inc(w_lo_ready, 1)

            def lo_result(i):
                g = groups[i]
                if g["piece"] is not None:
                    lo_piece(g["piece"] + W_AHEAD)
                if g["split_result"]:
                    hi, lo = split_result(g)
                    dve.wait_ge(taken, i + 1)
                    nc.vector.tensor_tensor(lo, result(i), hi.bitcast(F32), ALU.subtract).then_inc(lo_ready, 1)

            def indices():
                dve.wait_ge(cat_loaded, 16)
                nc.vector.tensor_scalar(wrap[:, :], cat_i[:, :], 0.0, float(V), ALU.is_lt, ALU.mult).then_inc(index_step, 1)
                dve.wait_ge(index_step, 1)
                nc.vector.tensor_tensor(row_f[:, :], cat_i[:, :], wrap[:, :], ALU.add).then_inc(index_step, 1)
                dve.wait_ge(index_step, 2)
                nc.vector.tensor_scalar(row_c[:, :], row_f[:, :], 0.0, float(V - 1), ALU.max, ALU.min).then_inc(index_step, 1)
                dve.wait_ge(base_ready, 1)
                dve.wait_ge(index_step, 3)
                nc.vector.tensor_tensor(row_index[:, :], row_c[:, :], table_base[:, :], ALU.add).then_inc(index_step, 1)

            def move_first(b):
                if b > 0:
                    dve.wait_ge(chunk_done, b * CHUNKS)
                dve.wait_ge(taken, n_bottom)
                nc.vector.tensor_copy(feats[:, :, :, 0].rearrange("d i s -> d s i"),
                                      bottom_full[:, b * TILE:(b + 1) * TILE].rearrange("d (s i) -> d s i", s=GROUP))\
                  .then_inc(first_moved, 1)

            def move_bank(u):
                b, j = divmod(u, BANKS)
                if u % 2 == 0:
                    return
                if b > 0:
                    dve.wait_ge(chunk_done, b * CHUNKS)
                dve.wait_ge(bank_turned, u + 1)
                w = len(bank_tables(j))
                f = 1 + j * BANK_TABLES
                nc.vector.tensor_copy(feats[:, :, :, f:f + w].rearrange("d i s n -> d n s i"),
                                      turned[:, u % 2, 0:w, :].rearrange("d n (s i) -> d n s i", s=GROUP))\
                  .then_inc(odd_moved, 1)

            def move_chunk(n):
                b, c = divmod(n, CHUNKS)
                if n == 0:
                    dve.wait_ge(mask_loaded, 16)
                for s in range(GROUP):
                    dve.wait_ge(a_moved, n * GROUP + s + 1)
                    src = dots[QUAD * s:QUAD * s + NF, n % 2, :, s * NF + WIN:(s + 1) * NF].rearrange("p i c -> p c i")
                    at = b * TILE + s * QUAD + c * CHUNK
                    for q in range(P // QUAD):
                        w = min(KT, WIN - q * KT)
                        last = nc.vector.copy_predicated(
                            pairs[QUAD * q:QUAD * q + NF, 0:w, at:at + CHUNK],
                            mask[QUAD * q:QUAD * q + NF, q * KT:q * KT + w, :],
                            src[:, q * KT:q * KT + w, :])
                last.then_inc(b_moved, 1)

            nc.vector.memset(x_dense, 0.0).then_inc(zeroed, 1)
            indices()
            nc.vector.memset(feats[:, :, :, NF:QUAD], 0.0).then_inc(zeroed, 1)
            for what, *n in work:
                if what == "group":
                    lo_result(*n)
                elif what == "first":
                    move_first(*n)
                elif what == "bank":
                    move_bank(*n)
                elif what == "chunk":
                    move_chunk(*n)
                elif what == "pieces":
                    for p in range(W_AHEAD):
                        lo_piece(p)


def first_top_rows():
    rows = np.full((KT, P), -1)
    free = np.ones((KT, P), bool)
    pair = {}
    for at, (i, j) in enumerate(zip(*np.triu_indices(NF, k=1))):
        pair[i, j] = pair[j, i] = E + at
    for k in range(SLOTS):
        t, q = k % KT, k // KT
        for r in range(NF if k < WIN else WIN):
            free[t, QUAD * q + r] = False
            c = NF - 1 if k == WIN else k if k < r <= k + WIN else k + WIN
            if r != k:
                rows[t, QUAD * q + r] = pair[r, c]
    places = np.argwhere(free)
    for n, (t, p) in zip([*range(E), TOP_PAD - 1], places):
        rows[t, p] = n
    assert sorted(rows[rows >= 0]) == list(range(TOP_PAD))
    return rows


def by_output_tile(w, kt):
    n = w.shape[1]
    return np.ascontiguousarray(w.reshape(kt, P, n // P, P).transpose(1, 2, 0, 3).reshape(P, -1))


def kernel(**inputs):
    import concourse.bacc as bacc
    from concourse.bass_utils import run_bass_kernel_spmd

    a = {k.replace("L0_rec_", ""): np.asarray(v) for k, v in inputs.items()}
    nc = bacc.Bacc("TRN2", target_bir_lowering=False, num_devices=1)
    arrays = {}

    def dram(name, x):
        arrays[name] = np.ascontiguousarray(x)
        return nc.dram_tensor(name, x.shape, mybir.dt.from_np(x.dtype), kind="ExternalInput").ap()

    rows = first_top_rows().ravel()
    tw0 = np.zeros((KT * P, a["tw0"].shape[1]), np.float32)
    tw0[rows >= 0] = a["tw0"][rows[rows >= 0]]
    tops = [tw0] + [a[f"tw{n}"] for n in (1, 2, 3)]
    is_bottom = (rows >= 0) & (rows < E)
    bw3 = np.zeros((a["bw2"].shape[0], KT * P), np.float32)
    bw3[:, is_bottom] = a["bw2"][:, rows[is_bottom]]
    bb3 = np.zeros(KT * P, np.float32)
    bb3[is_bottom] = a["bb2"][rows[is_bottom]]
    bw0 = np.zeros((P, BOTTOM[0][1] * P), np.float32)
    bw0[0:PAD_DENSE] = a["bw0"]
    bottom_w = np.concatenate([bw0, by_output_tile(a["bw1"], 4), by_output_tile(a["bw2"], 2), by_output_tile(bw3, 2)],
                              axis=1)
    biases = [a["bb0"], a["bb1"], a["bb2"], bb3, a["tb0"], a["tb1"], a["tb2"], a["tb3"]]
    b_mask = np.ones((P, WIN, CHUNK), np.uint32)
    for q in range(P // QUAD):
        for k in range(WIN):
            b_mask[QUAD * q + k + 1:QUAD * q + k + 1 + WIN, k] = 0
    args = [
        dram("cat", a["r_cat_features"].reshape(TILES, TILE, T).transpose(1, 0, 2).reshape(TILE, TILES * T)),
        dram("dense", a["r_numerical"].T),
        dram("emb", a["emb_tables"].reshape(T * V, E)),
        dram("bottom_w", bottom_w),
        [dram(f"top_w{n}", by_output_tile(w, TOP[n][0])) for n, w in enumerate(tops)],
        dram("last_w", a["tw4"].reshape(2, P).T),
        dram("biases", np.concatenate([x.reshape(-1, P).T for x in biases], axis=1)),
        dram("last_bias", a["tb4"].reshape(1, 1)),
        dram("identity", np.eye(P, dtype=np.float32)),
        dram("b_mask", b_mask),
    ]
    out = nc.dram_tensor("out", (B, 1), F32, kind="ExternalOutput").ap()
    dlrm(nc, *args, out.rearrange("b o -> o b"))
    r = run_bass_kernel_spmd(nc, [arrays], core_ids=[0])
    return r.results[0]["out"]
```

```python
from contextlib import ExitStack

import concourse.bass as bass
import numpy as np
from concourse import mybir

F32 = mybir.dt.float32
F32R = mybir.dt.float32r
I32 = mybir.dt.int32
U32 = mybir.dt.uint32
ALU = mybir.AluOpType
ACT = mybir.ActivationFunctionType

P = 128
B = 512
E = 128
T = 26
V = 12500
NF = T + 1
NUM_DENSE, PAD_DENSE = 13, 16
TILE = 128
TILES = B // TILE
HALF = 256
HALVES = B // HALF
TOP_PAD = 480

QUAD = 32
WIN = NF // 2
SLOTS = WIN + 1
KT = 4

BOTTOM = [(1, 4), (4, 2), (2, 1), (2, KT)]
TOP = [(KT, 8), (8, 8), (8, 4), (4, 2)]
LAYERS = BOTTOM + TOP + [(2, 1)]
TOP0, TOP1, TOP2, TOP3, LAST = range(len(BOTTOM), len(LAYERS))
BIAS_COLS = [sum(mt for _, mt in LAYERS[:n]) for n in range(len(LAYERS))]

BANK_TABLES = 4
BANKS = -(-T // BANK_TABLES)
GROUP = P // QUAD
DOT_ROWS = (GROUP - 1) * QUAD + NF
CHUNK = 8
CHUNKS = TILE // (GROUP * CHUNK)

W_RING = 4
W_AHEAD = W_RING - 1
ROW_RING = 36
PIECE = 1024

LOADS = [(0, m, 2) for m in range(0, 8, 2)] + [(1, m, 1) for m in range(8)] + [(2, m, 1) for m in range(4)] + [(3, 0, 2)]


def bank_tables(bank):
    return range(bank * BANK_TABLES, min(T, (bank + 1) * BANK_TABLES))


def order():
    groups, pieces, work = [], [], []

    def group(layer, m, at, n, split):
        piece = None
        if split:
            piece = len(pieces)
            pieces.append(dict(layer=layer, m=m, group=len(groups)))
        groups.append(dict(layer=layer, m=m, at=at, n=n, piece=piece,
                           split_result=layer == TOP1 or (split and layer < TOP3)))
        return ("group", len(groups) - 1)

    def layer(n, at, cols, split=False):
        return [group(n, m, at, cols, split) for m in range(LAYERS[n][1])]

    main = [x for n in range(len(BOTTOM)) for x in layer(n, 0, B)]
    for tile in range(2):
        main += layer(TOP0, tile * TILE, TILE) + layer(TOP1, tile * TILE, TILE)
    main += layer(TOP2, 0, HALF, True) + layer(TOP3, 0, HALF, True) + layer(LAST, 0, HALF)
    for n in (TOP0, TOP1, TOP2, TOP3):
        main += layer(n, HALF, HALF, True)
    main += layer(LAST, HALF, HALF)

    side = []
    for b, (first, banks, chunks, pairs) in enumerate(TILE_PLACES):
        side.append((first, ("first", b)))
        side += [(at, ("bank", b * BANKS + j)) for j, at in enumerate(banks)]
        side += [(at, ("chunk", b * CHUNKS + c)) for c, at in enumerate(chunks)]
        side += [(at, ("pairs", b)) for at in pairs]
    side += [(at, ("piece", n)) for n, at in enumerate(PIECE_PLACES)]
    side.sort(key=lambda x: x[0])
    for at, x in enumerate(main):
        work += [y for place, y in side if place == at] + [x]
    return groups, pieces, work


TILE_PLACES = [
    (9, [5, 5, 5, 7, 10, 11, 11], [11, 11, 11, 11], []),
    (15, [11, 11, 13, 20, 22, 23, 24], [25, 25, 26, 26], []),
    (28, [26, 27, 30, 31, 35, 39, 40], [41, 41, 43, 43], [45]),
    (44, [41, 43, 44, 44, 46, 47, 47], [48, 48, 48, 48], [49]),
]
PIECE_PLACES = [29, 36, 37]


def dlrm(nc, cat, dense, emb, bottom_w, top_w, last_w, biases, last_bias, identity, b_mask, out):
    groups, pieces, work = order()
    n_bottom = sum(mt for _, mt in BOTTOM)

    def split_results(i):
        return sum(g["split_result"] for g in groups[:i])

    def writer(g, k, i):
        source = 1 if g["layer"] == 3 else g["layer"] - 1
        return max(n for n in range(i) if groups[n]["layer"] == source and groups[n]["m"] == k)

    ctx = ExitStack()
    with ctx:
        def sb(name, shape, dt=F32):
            return ctx.enter_context(nc.sbuf_tensor(name, shape, dt))

        def sem(name):
            return ctx.enter_context(nc.semaphore(name))

        cat_i = sb("cat_i", [P, TILES * T], I32)
        wrap = sb("wrap", [P, TILES * T])
        row_f = sb("row_f", [P, TILES * T])
        table_base = sb("table_base", [P, TILES * T], I32)
        row_index = sb("row_index", [P, TILES * T], U32)
        rows = sb("rows", [P, ROW_RING, E])
        ident = sb("ident", [P, P])
        mask = sb("mask", [P, WIN, CHUNK], U32)
        bias = sb("bias", [P, BIAS_COLS[LAST]])
        bias_last = sb("bias_last", [1, 1])
        feats = sb("feats", [P, QUAD, GROUP, QUAD])
        bottom_full = sb("bottom_full", [P, B])
        x_dense = bottom_full[0:PAD_DENSE, :]
        pairs = sb("pairs", [P, KT, B])
        pairs_hi = sb("pairs_hi", [P, KT, HALF], F32R)
        pairs_lo = sb("pairs_lo", [P, KT, HALF], F32R)
        plain = sb("plain", [P, 8 * TILE])
        logits = plain[0:1, 0:B]
        split_of = {n: [sb(f"top{n - TOP0}_{part}", [P, LAYERS[n][1] * HALF], F32R) for part in ("hi", "lo")]
                    for n in (TOP0, TOP1, TOP2)}
        full = sb("full", [P, 2, HALF])
        last_x = sb("last_x", [P, 2, HALF])
        raw = [sb(f"raw{n}", [P, mt * kt * P]) for n, (kt, mt) in enumerate(TOP)]
        raw_last = sb("raw_last", [P, 2])
        w_hi = sb("w_hi", [P, W_RING, PIECE], F32R)
        w_lo = sb("w_lo", [P, W_RING, PIECE], F32R)

        bottom_at = [sum(kt * mt * P for kt, mt in BOTTOM[:n]) for n in range(len(BOTTOM) + 1)]
        raw_bottom = raw[2]

        turned = ctx.enter_context(nc.psum_tensor("turned", [P, 2, BANK_TABLES, TILE], F32))
        dots = ctx.enter_context(nc.psum_tensor("dots", [P, 2, CHUNK, P], F32))
        acc = ctx.enter_context(nc.psum_tensor("acc", [P, 2, B], F32))

        cat_loaded, dense_loaded, bias_loaded = sem("cat_loaded"), sem("dense_loaded"), sem("bias_loaded")
        ident_loaded, mask_loaded = sem("ident_loaded"), sem("mask_loaded")
        bottom_loaded = [sem(f"bottom{n}_loaded") for n in range(len(BOTTOM))]
        top_loaded = [sem(f"top{n}_{m}_loaded") for n, m, _ in LOADS]
        last_loaded, bias_last_loaded = sem("last_loaded"), sem("bias_last_loaded")
        gathered = [sem(f"gathered{u}") for u in range(TILES * BANKS)]
        stored = sem("stored")
        base_ready = sem("base_ready")
        index_step = sem("index_step")
        zeroed = sem("zeroed")
        w_hi_ready, w_lo_ready = sem("w_hi_ready"), sem("w_lo_ready")
        group_done = sem("group_done")
        taken = sem("taken")
        lo_ready = sem("lo_ready")
        bank_turned = sem("bank_turned")
        even_moved, odd_moved = sem("even_moved"), sem("odd_moved")
        first_moved = sem("first_moved")
        chunk_done = sem("chunk_done")
        a_moved = sem("a_moved")
        b_moved = sem("b_moved")
        pairs_hi_ready, pairs_lo_ready = sem("pairs_hi_ready"), sem("pairs_lo_ready")

        def result(i):
            g = groups[i]
            layer, m, at, n = g["layer"], g["m"], g["at"], g["n"]
            if g["split_result"]:
                return full[:, split_results(i) % 2, 0:n]
            if layer == 2:
                return bottom_full[:, :]
            if layer in (0, 3):
                return pairs[:, m, :]
            if layer in (1, TOP0):
                return plain[:, m * n:(m + 1) * n]
            assert layer == TOP3
            return last_x[:, m, :]

        def split_result(g):
            hi, lo = split_of[g["layer"]]
            c = g["m"] * HALF + g["at"] % HALF
            return hi[:, c:c + g["n"]], lo[:, c:c + g["n"]]

        def plain_x(g, k):
            layer, at, n = g["layer"], g["at"], g["n"]
            if layer == 0:
                return x_dense
            if layer in (1, TOP0):
                return pairs[:, k, at:at + n]
            if layer == LAST:
                return last_x[:, k, :]
            return plain[:, k * n:(k + 1) * n]

        def split_x(g, k):
            if g["layer"] == TOP0:
                return pairs_hi[:, k, :], pairs_lo[:, k, :]
            hi, lo = split_of[g["layer"] - 1]
            return hi[:, k * HALF:(k + 1) * HALF], lo[:, k * HALF:(k + 1) * HALF]

        def weights(layer, m):
            kt = LAYERS[layer][0]
            if layer < len(BOTTOM):
                at = bottom_at[layer] + m * kt * P
                return raw_bottom[0:PAD_DENSE if layer == 0 else P, at:at + kt * P]
            if layer == LAST:
                return raw_last[:, :]
            return raw[layer - TOP0][:, m * kt * P:(m + 1) * kt * P]

        def weights_loaded(eng, layer, m):
            if layer < len(BOTTOM):
                eng.wait_ge(bottom_loaded[layer], 16)
            elif layer == LAST:
                eng.wait_ge(last_loaded, 16)
            else:
                load = next(x for x, (n, first, count) in enumerate(LOADS)
                            if n == layer - TOP0 and first <= m < first + count)
                eng.wait_ge(top_loaded[load], 16)

        block = ctx.enter_context(nc.Block())

        @block.sync
        def _(sp):
            sp.dma_start(cat_i[:, :], cat).then_inc(cat_loaded, 16)
            sp.wait_ge(zeroed, 1)
            sp.dma_start(x_dense[0:NUM_DENSE, :], dense).then_inc(dense_loaded, 16)
            for n in range(len(BOTTOM)):
                parts = PAD_DENSE if n == 0 else P
                c = slice(bottom_at[n], bottom_at[n + 1])
                sp.dma_start(raw_bottom[0:parts, c], bottom_w[0:parts, c]).then_inc(bottom_loaded[n], 16)
                if n == 0:
                    sp.dma_start(bias[:, :], biases).then_inc(bias_loaded, 16)
            sp.dma_start(ident[:, :], identity).then_inc(ident_loaded, 16)
            sp.dma_start(mask[:, :, :], b_mask).then_inc(mask_loaded, 16)
            for x, (n, m, count) in enumerate(LOADS):
                if x >= 2:
                    sp.wait_ge(gathered[x - 2], 16 * len(bank_tables((x - 2) % BANKS)))
                if (n, m) == (2, 0):
                    sp.wait_ge(group_done, n_bottom)
                size = TOP[n][0] * P
                c = slice(m * size, (m + count) * size)
                sp.dma_start(raw[n][:, c], top_w[n][:, c]).then_inc(top_loaded[x], 16)
            sp.dma_start(raw_last[:, :], last_w).then_inc(last_loaded, 16)
            sp.dma_start(bias_last[:, :], last_bias).then_inc(bias_last_loaded, 16)
            sp.wait_ge(taken, len(groups))
            sp.dma_start(out, logits).then_inc(stored, 16)
            sp.wait_ge(stored, 16)

        @block.gpsimd
        def _(pool):
            nc.gpsimd.iota(table_base[:, :].rearrange("p (b t) -> p b t", b=TILES),
                           pattern=[[0, TILES], [V, T]], base=0, channel_multiplier=0).then_inc(base_ready, 1)
            pool.wait_ge(index_step, 3)
            for b in range(TILES):
                for j in range(BANKS):
                    last = b * T + max(bank_tables(j)) - ROW_RING
                    if last >= 0:
                        pool.wait_ge(bank_turned, last // T * BANKS + last % T // BANK_TABLES + 1)
                    for t in bank_tables(j):
                        c = b * T + t
                        pool.indirect_dma_start(
                            rows[:, c % ROW_RING, :], None, emb,
                            bass.IndirectOffsetOnAxis(ap=row_index[:, c:c + 1], axis=0),
                        ).then_inc(gathered[b * BANKS + j], 16)

        @block.tensor
        def _(pe):
            def plain_group(i):
                g = groups[i]
                kt = LAYERS[g["layer"]][0]
                w = weights(g["layer"], g["m"])
                cols = P if g["layer"] < LAST else 1
                weights_loaded(pe, g["layer"], g["m"])
                if g["layer"] == 0:
                    pe.wait_ge(dense_loaded, 16)
                if i >= 2:
                    pe.wait_ge(taken, i - 1)
                if g["layer"] == TOP0:
                    pe.wait_ge(b_moved, (g["at"] // TILE + 1) * CHUNKS)
                for k in range(kt):
                    if g["m"] == 0 and g["layer"] not in (0, TOP0):
                        pe.wait_ge(taken, writer(g, k, i) + 1)
                    mm = pe.matmul(acc[0:cols, i % 2, 0:g["n"]], w[:, k * cols:(k + 1) * cols], plain_x(g, k),
                                   start=k == 0, stop=k == kt - 1)
                mm.then_inc(group_done, 1)

            def split_group(i):
                g = groups[i]
                kt = LAYERS[g["layer"]][0]
                slot = g["piece"] % W_RING
                pe.wait_ge(w_hi_ready, g["piece"] + 1)
                pe.wait_ge(w_lo_ready, g["piece"] + 1)
                pe.wait_ge(taken, i - 1)
                if g["layer"] == TOP0:
                    pe.wait_ge(pairs_hi_ready, 2)
                    pe.wait_ge(pairs_lo_ready, 2)
                for k in range(kt):
                    hi, lo = split_x(g, k)
                    wh = w_hi[:, slot, k * P:(k + 1) * P]
                    wl = w_lo[:, slot, k * P:(k + 1) * P]
                    if g["m"] == 0 and g["layer"] > TOP0:
                        pe.wait_ge(taken, writer(g, k, i) + 1)
                    pe.matmul(acc[:, i % 2, 0:HALF], wh, hi, start=k == 0, stop=False)
                    pe.matmul(acc[:, i % 2, 0:HALF], wl, hi, start=False, stop=False)
                    if g["m"] == 0 and g["layer"] > TOP0:
                        pe.wait_ge(lo_ready, split_results(writer(g, k, i) + 1))
                    mm = pe.matmul(acc[:, i % 2, 0:HALF], wh, lo, start=False, stop=k == kt - 1)
                mm.then_inc(group_done, 1)

            def bank(u):
                b, j = divmod(u, BANKS)
                pe.wait_ge(gathered[u], 16 * len(bank_tables(j)))
                if u == 0:
                    pe.wait_ge(ident_loaded, 16)
                if u >= 2:
                    pe.wait_ge(odd_moved if u % 2 else even_moved, u // 2)
                for t in bank_tables(j):
                    tr = pe.transpose(turned[:, u % 2, t % BANK_TABLES, :], rows[:, (b * T + t) % ROW_RING, :], ident[:, :])
                tr.then_inc(bank_turned, 1)

            def chunk(n):
                b, c = divmod(n, CHUNKS)
                if c == 0:
                    done = (b + 1) * BANKS
                    pe.wait_ge(even_moved, (done + 1) // 2)
                    pe.wait_ge(odd_moved, done // 2)
                    pe.wait_ge(first_moved, b + 1)
                if n >= 2:
                    pe.wait_ge(b_moved, n - 1)
                for x in range(CHUNK):
                    i = c * CHUNK + x
                    mm = pe.matmul(dots[0:DOT_ROWS, n % 2, x, 0:GROUP * NF],
                                   feats[:, i, :, :].rearrange("p s f -> p (s f)")[:, 0:DOT_ROWS], feats[:, i, :, 0:NF],
                                   start=True, stop=True)
                mm.then_inc(chunk_done, 1)

            for what, *n in work:
                if what == "group" and groups[n[0]]["piece"] is None:
                    plain_group(*n)
                elif what == "group":
                    split_group(*n)
                elif what == "bank":
                    bank(*n)
                elif what == "chunk":
                    chunk(*n)

        @block.scalar
        def _(act):
            def split_piece(n):
                if n >= len(pieces):
                    return
                p = pieces[n]
                size = LAYERS[p["layer"]][0] * P
                weights_loaded(act, p["layer"], p["m"])
                if n >= W_RING:
                    act.wait_ge(group_done, pieces[n - W_RING]["group"] + 1)
                    act.wait_ge(w_lo_ready, n - W_RING + 1)
                nc.scalar.copy(w_hi[:, n % W_RING, 0:size], weights(p["layer"], p["m"])).then_inc(w_hi_ready, 1)

            def take(i):
                g = groups[i]
                n = g["n"]
                if g["piece"] is not None:
                    split_piece(g["piece"] + W_AHEAD)
                act.wait_ge(group_done, i + 1)
                if g["layer"] == LAST:
                    act.wait_ge(bias_last_loaded, 16)
                    nc.scalar.activation(logits[:, g["at"]:g["at"] + n], acc[0:1, i % 2, 0:n],
                                         ACT.Identity, bias=bias_last[:, 0:1]).then_inc(taken, 1)
                    return
                if i == 0:
                    act.wait_ge(bias_loaded, 16)
                col = BIAS_COLS[g["layer"]] + g["m"]
                if g["split_result"]:
                    if split_results(i) >= 2:
                        act.wait_ge(lo_ready, split_results(i) - 1)
                    nc.scalar.activation(split_result(g)[0], acc[:, i % 2, 0:n], ACT.Relu, bias=bias[:, col:col + 1])
                nc.scalar.activation(result(i), acc[:, i % 2, 0:n], ACT.Relu, bias=bias[:, col:col + 1])\
                  .then_inc(taken, 1)

            def move_bank(u):
                b, j = divmod(u, BANKS)
                if u % 2:
                    return
                if b > 0:
                    act.wait_ge(chunk_done, b * CHUNKS)
                act.wait_ge(bank_turned, u + 1)
                if u == 0:
                    act.wait_ge(zeroed, 2)
                w = len(bank_tables(j))
                f = 1 + j * BANK_TABLES
                nc.scalar.copy(feats[:, :, :, f:f + w].rearrange("d i s n -> d n s i"),
                               turned[:, u % 2, 0:w, :].rearrange("d n (s i) -> d n s i", s=GROUP))\
                  .then_inc(even_moved, 1)

            def move_chunk(n):
                b, c = divmod(n, CHUNKS)
                act.wait_ge(chunk_done, n + 1)
                for s in range(GROUP):
                    src = dots[QUAD * s:QUAD * s + NF, n % 2, :, s * NF:(s + 1) * NF].rearrange("p i c -> p c i")
                    at = b * TILE + s * QUAD + c * CHUNK
                    for q in range(3):
                        nc.scalar.copy(pairs[QUAD * q:QUAD * q + NF, :, at:at + CHUNK], src[:, q * KT:(q + 1) * KT, :])
                    nc.scalar.copy(pairs[QUAD * 3:QUAD * 3 + NF, 0, at:at + CHUNK], src[:, 3 * KT, :])
                    nc.scalar.copy(pairs[QUAD * 3:QUAD * 3 + WIN, 1, at:at + CHUNK], src[0:WIN, NF - 1, :])\
                      .then_inc(a_moved, 1)

            def split_pairs(b):
                act.wait_ge(b_moved, (b + 1) * CHUNKS)
                c = b % 2 * TILE
                nc.scalar.copy(pairs_hi[:, :, c:c + TILE], pairs[:, :, b * TILE:(b + 1) * TILE]).then_inc(pairs_hi_ready, 1)

            for what, *n in work:
                if what == "group":
                    take(*n)
                elif what == "pairs":
                    split_pairs(*n)
                elif what == "bank":
                    move_bank(*n)
                elif what == "chunk":
                    move_chunk(*n)
                elif what == "piece":
                    split_piece(*n)

        @block.vector
        def _(dve):
            def lo_piece(n):
                if n >= len(pieces):
                    return
                p = pieces[n]
                size = LAYERS[p["layer"]][0] * P
                if n >= W_RING:
                    dve.wait_ge(group_done, pieces[n - W_RING]["group"] + 1)
                dve.wait_ge(w_hi_ready, n + 1)
                nc.vector.tensor_tensor(w_lo[:, n % W_RING, 0:size], weights(p["layer"], p["m"]),
                                        w_hi[:, n % W_RING, 0:size].bitcast(F32), ALU.subtract)\
                  .then_inc(w_lo_ready, 1)

            def lo_result(i):
                g = groups[i]
                if g["piece"] is not None:
                    lo_piece(g["piece"] + W_AHEAD)
                if g["split_result"]:
                    hi, lo = split_result(g)
                    dve.wait_ge(taken, i + 1)
                    nc.vector.tensor_tensor(lo, result(i), hi.bitcast(F32), ALU.subtract).then_inc(lo_ready, 1)

            def indices():
                dve.wait_ge(cat_loaded, 16)
                nc.vector.tensor_scalar(wrap[:, :], cat_i[:, :], 0.0, float(V), ALU.is_lt, ALU.mult).then_inc(index_step, 1)
                dve.wait_ge(index_step, 1)
                nc.vector.scalar_tensor_tensor(out=row_f[:, :], in0=cat_i[:, :], scalar=float(V - 1), in1=wrap[:, :],
                                               op0=ALU.min, op1=ALU.add).then_inc(index_step, 1)
                dve.wait_ge(base_ready, 1)
                dve.wait_ge(index_step, 2)
                nc.vector.scalar_tensor_tensor(out=row_index[:, :], in0=row_f[:, :], scalar=0.0, in1=table_base[:, :],
                                               op0=ALU.max, op1=ALU.add).then_inc(index_step, 1)

            def move_first(b):
                if b > 0:
                    dve.wait_ge(chunk_done, b * CHUNKS)
                dve.wait_ge(taken, n_bottom)
                nc.vector.tensor_copy(feats[:, :, :, 0].rearrange("d i s -> d s i"),
                                      bottom_full[:, b * TILE:(b + 1) * TILE].rearrange("d (s i) -> d s i", s=GROUP))\
                  .then_inc(first_moved, 1)

            def move_bank(u):
                b, j = divmod(u, BANKS)
                if u % 2 == 0:
                    return
                if b > 0:
                    dve.wait_ge(chunk_done, b * CHUNKS)
                dve.wait_ge(bank_turned, u + 1)
                w = len(bank_tables(j))
                f = 1 + j * BANK_TABLES
                nc.vector.tensor_copy(feats[:, :, :, f:f + w].rearrange("d i s n -> d n s i"),
                                      turned[:, u % 2, 0:w, :].rearrange("d n (s i) -> d n s i", s=GROUP))\
                  .then_inc(odd_moved, 1)

            def move_chunk(n):
                b, c = divmod(n, CHUNKS)
                if n == 0:
                    dve.wait_ge(mask_loaded, 16)
                for s in range(GROUP):
                    dve.wait_ge(a_moved, n * GROUP + s + 1)
                    src = dots[QUAD * s:QUAD * s + NF, n % 2, :, s * NF + WIN:(s + 1) * NF].rearrange("p i c -> p c i")
                    at = b * TILE + s * QUAD + c * CHUNK
                    for q in range(P // QUAD):
                        w = min(KT, WIN - q * KT)
                        last = nc.vector.copy_predicated(
                            pairs[QUAD * q:QUAD * q + NF, 0:w, at:at + CHUNK],
                            mask[QUAD * q:QUAD * q + NF, q * KT:q * KT + w, :],
                            src[:, q * KT:q * KT + w, :])
                last.then_inc(b_moved, 1)

            def lo_pairs(b):
                dve.wait_ge(pairs_hi_ready, b - 1)
                c = b % 2 * TILE
                nc.vector.tensor_tensor(pairs_lo[:, :, c:c + TILE], pairs[:, :, b * TILE:(b + 1) * TILE],
                                        pairs_hi[:, :, c:c + TILE].bitcast(F32), ALU.subtract)\
                  .then_inc(pairs_lo_ready, 1)

            nc.vector.memset(x_dense, 0.0).then_inc(zeroed, 1)
            indices()
            nc.vector.memset(feats[:, :, :, NF:QUAD], 0.0).then_inc(zeroed, 1)
            for what, *n in work:
                if what == "group":
                    lo_result(*n)
                elif what == "pairs":
                    lo_pairs(*n)
                elif what == "first":
                    move_first(*n)
                elif what == "bank":
                    move_bank(*n)
                elif what == "chunk":
                    move_chunk(*n)
                elif what == "piece":
                    lo_piece(*n)


def first_top_rows():
    rows = np.full((KT, P), -1)
    free = np.ones((KT, P), bool)
    pair = {}
    for at, (i, j) in enumerate(zip(*np.triu_indices(NF, k=1))):
        pair[i, j] = pair[j, i] = E + at
    for k in range(SLOTS):
        t, q = k % KT, k // KT
        for r in range(NF if k < WIN else WIN):
            free[t, QUAD * q + r] = False
            c = NF - 1 if k == WIN else k if k < r <= k + WIN else k + WIN
            if r != k:
                rows[t, QUAD * q + r] = pair[r, c]
    places = np.argwhere(free)
    for n, (t, p) in zip([*range(E), TOP_PAD - 1], places):
        rows[t, p] = n
    assert sorted(rows[rows >= 0]) == list(range(TOP_PAD))
    return rows


def by_output_tile(w, kt):
    n = w.shape[1]
    return np.ascontiguousarray(w.reshape(kt, P, n // P, P).transpose(1, 2, 0, 3).reshape(P, -1))


def kernel(**inputs):
    import concourse.bacc as bacc
    from concourse.bass_utils import run_bass_kernel_spmd

    a = {k.replace("L0_rec_", ""): np.asarray(v) for k, v in inputs.items()}
    nc = bacc.Bacc("TRN2", target_bir_lowering=False, num_devices=1)
    arrays = {}

    def dram(name, x):
        arrays[name] = np.ascontiguousarray(x)
        return nc.dram_tensor(name, x.shape, mybir.dt.from_np(x.dtype), kind="ExternalInput").ap()

    rows = first_top_rows().ravel()
    tw0 = np.zeros((KT * P, a["tw0"].shape[1]), np.float32)
    tw0[rows >= 0] = a["tw0"][rows[rows >= 0]]
    tops = [tw0] + [a[f"tw{n}"] for n in (1, 2, 3)]
    is_bottom = (rows >= 0) & (rows < E)
    bw3 = np.zeros((a["bw2"].shape[0], KT * P), np.float32)
    bw3[:, is_bottom] = a["bw2"][:, rows[is_bottom]]
    bb3 = np.zeros(KT * P, np.float32)
    bb3[is_bottom] = a["bb2"][rows[is_bottom]]
    bw0 = np.zeros((P, BOTTOM[0][1] * P), np.float32)
    bw0[0:PAD_DENSE] = a["bw0"]
    bottom_w = np.concatenate([bw0, by_output_tile(a["bw1"], 4), by_output_tile(a["bw2"], 2), by_output_tile(bw3, 2)],
                              axis=1)
    biases = [a["bb0"], a["bb1"], a["bb2"], bb3, a["tb0"], a["tb1"], a["tb2"], a["tb3"]]
    b_mask = np.ones((P, WIN, CHUNK), np.uint32)
    for q in range(P // QUAD):
        for k in range(WIN):
            b_mask[QUAD * q + k + 1:QUAD * q + k + 1 + WIN, k] = 0
    args = [
        dram("cat", a["r_cat_features"].reshape(TILES, TILE, T).transpose(1, 0, 2).reshape(TILE, TILES * T)),
        dram("dense", a["r_numerical"].T),
        dram("emb", a["emb_tables"].reshape(T * V, E)),
        dram("bottom_w", bottom_w),
        [dram(f"top_w{n}", by_output_tile(w, TOP[n][0])) for n, w in enumerate(tops)],
        dram("last_w", a["tw4"].reshape(2, P).T),
        dram("biases", np.concatenate([x.reshape(-1, P).T for x in biases], axis=1)),
        dram("last_bias", a["tb4"].reshape(1, 1)),
        dram("identity", np.eye(P, dtype=np.float32)),
        dram("b_mask", b_mask),
    ]
    out = nc.dram_tensor("out", (B, 1), F32, kind="ExternalOutput").ap()
    dlrm(nc, *args, out.rearrange("b o -> o b"))
    r = run_bass_kernel_spmd(nc, [arrays], core_ids=[0])
    return r.results[0]["out"]
```
